# Optimizing a Trainium2 kernel written in Bass

```python
import numpy as np
import jax
import jax.numpy as jnp

def _softmax(x, axis=-1):
    return jax.nn.softmax(x, axis=axis)

def _gelu(x):
    return jax.nn.gelu(x, approximate=True)

def _silu(x):
    return jax.nn.silu(x)

def _sigmoid(x):
    return jax.nn.sigmoid(x)

def _layernorm(x, axis=-1, eps=1e-05):
    m = jnp.mean(x, axis=axis, keepdims=True)
    v = jnp.var(x, axis=axis, keepdims=True)
    return (x - m) / jnp.sqrt(v + eps)

def _scatter_add(tgt, idx, src, axis=0):
    return tgt.at[idx].add(src)

def _segment_sum(src, seg, n):
    return jax.ops.segment_sum(src, seg, n)
kernel_name = 'mk_vit_tower_cls_d1_tok_img1024_r4_4e6a0e'

def setup_inputs(seed: int=0):
    np.random.seed(seed)
    _w = jnp.asarray

    def _rec_inputs():
        import jax
        import jax.numpy as jnp
        _rk = jax.random.key(seed)
        x = -0.00016672 + 0.999947 * jax.random.normal(jax.random.fold_in(_rk, 1), (64, 3, 96, 96), jnp.float32)
        cls_tok = 0.02 * jax.random.normal(jax.random.fold_in(_rk, 5), (1, 1, 256), jnp.float32)
        return (x, cls_tok)
    x, cls_tok = _rec_inputs()

    def _L0_tok_setup():
        import jax, jax.numpy as jnp
        import numpy as np
        DIM = 256
        IMG = 96
        P = 16
        C = 3
        TEMP = 10000.0
        EPS = 1e-05
        PATCH_DIM = C * P * P
        HP = IMG // P

        def layernorm(x, gamma, beta):
            mu = jnp.mean(x, axis=-1, keepdims=True)
            var = jnp.var(x, axis=-1, keepdims=True)
            return (x - mu) * jax.lax.rsqrt(var + EPS) * gamma + beta

        def posemb_sincos_2d(h, w, dim, dtype):
            y, x = jnp.meshgrid(jnp.arange(h), jnp.arange(w), indexing='ij')
            omega = jnp.arange(dim // 4, dtype=jnp.float32) / (dim // 4 - 1)
            omega = 1.0 / TEMP ** omega
            y = y.reshape(-1)[:, None] * omega[None, :]
            x = x.reshape(-1)[:, None] * omega[None, :]
            pe = jnp.concatenate((jnp.sin(x), jnp.cos(x), jnp.sin(y), jnp.cos(y)), axis=1)
            return pe.astype(dtype)
        key = jax.random.key(seed)
        ks = jax.random.split(key, 8)
        B = 64
        img = jax.random.normal(ks[0], (B, C, IMG, IMG), dtype=jnp.float32)
        cls_token = jax.random.normal(ks[1], (1, 1, DIM), dtype=jnp.float32)
        cls_pos_embedding = jax.random.normal(ks[2], (1, 1, DIM), dtype=jnp.float32)
        ln1_g = jnp.ones((PATCH_DIM,), jnp.float32)
        ln1_b = jnp.zeros((PATCH_DIM,), jnp.float32)
        W = jax.random.normal(ks[3], (PATCH_DIM, DIM), dtype=jnp.float32) / np.sqrt(PATCH_DIM)
        bias = jnp.zeros((DIM,), jnp.float32)
        ln2_g = jnp.ones((DIM,), jnp.float32)
        ln2_b = jnp.zeros((DIM,), jnp.float32)
        return {'img': img, 'cls_token': cls_token, 'cls_pos_embedding': cls_pos_embedding, 'ln1_g': ln1_g, 'ln1_b': ln1_b, 'W': W, 'bias': bias, 'ln2_g': ln2_g, 'ln2_b': ln2_b}
    _L0_tok_all = _L0_tok_setup()
    _L0_tok_in = {k: v for k, v in _L0_tok_all.items() if k in ('cls_token', 'cls_pos_embedding', 'ln1_g', 'ln1_b', 'W', 'bias', 'ln2_g', 'ln2_b')}
    del _L0_tok_all

    def _L0_attn_setup():
        import jax, jax.numpy as jnp
        import numpy as np
        HEADS = 8
        K_SIZE = 64
        key = jax.random.key(seed)
        k1, k2, k3, k4 = jax.random.split(key, 4)
        B, C, D = (4, 512, 256)
        return {'x': jax.random.normal(k1, (B, C, D), dtype=jnp.float32), 'Mq': jax.random.normal(k2, (D, HEADS * K_SIZE), dtype=jnp.float32) * 0.02, 'Mk': jax.random.normal(k3, (D, HEADS * K_SIZE), dtype=jnp.float32) * 0.02, 'Mv': jax.random.normal(k4, (D, 256), dtype=jnp.float32) * 0.02}
    _L0_attn_all = _L0_attn_setup()
    _L0_attn_in = {k: v for k, v in _L0_attn_all.items() if k in ('Mq', 'Mk', 'Mv')}
    del _L0_attn_all

    def _L0_ffn_setup():
        import jax, jax.numpy as jnp
        import numpy as np
        H, I, E_ROUTED, TOP_K = (256, 704, 7, 2)
        B, S = (4, 512)

        def _expert(h, g, u, d):
            return jnp.einsum('...i,hi->...h', jax.nn.silu(h @ g.T) * (h @ u.T), d)
        key = jax.random.key(seed)
        ks = jax.random.split(key, 10)
        sc = 0.02
        return {'x': jax.random.normal(ks[0], (B, S, H), dtype=jnp.float32), 'sg': jax.random.normal(ks[1], (I, H), dtype=jnp.float32) * sc, 'su': jax.random.normal(ks[2], (I, H), dtype=jnp.float32) * sc, 'sd': jax.random.normal(ks[3], (H, I), dtype=jnp.float32) * sc, 'rg': jax.random.normal(ks[4], (E_ROUTED, I, H), dtype=jnp.float32) * sc, 'ru': jax.random.normal(ks[5], (E_ROUTED, I, H), dtype=jnp.float32) * sc, 'rd': jax.random.normal(ks[6], (E_ROUTED, H, I), dtype=jnp.float32) * sc, 'wr': jax.random.normal(ks[7], (E_ROUTED, H), dtype=jnp.float32) * sc, 'rb': jnp.zeros((E_ROUTED,), dtype=jnp.float32)}
    _L0_ffn_all = _L0_ffn_setup()
    _L0_ffn_in = {k: v for k, v in _L0_ffn_all.items() if k in ('sg', 'su', 'sd', 'rg', 'ru', 'rd', 'wr', 'rb')}
    del _L0_ffn_all
    return {'x': x, 'cls_tok': cls_tok, 'L0_tok_cls_token': _L0_tok_in['cls_token'], 'L0_tok_cls_pos_embedding': _L0_tok_in['cls_pos_embedding'], 'L0_tok_ln1_g': _L0_tok_in['ln1_g'], 'L0_tok_ln1_b': _L0_tok_in['ln1_b'], 'L0_tok_W': _L0_tok_in['W'], 'L0_tok_bias': _L0_tok_in['bias'], 'L0_tok_ln2_g': _L0_tok_in['ln2_g'], 'L0_tok_ln2_b': _L0_tok_in['ln2_b'], 'L0_attn_Mq': _L0_attn_in['Mq'], 'L0_attn_Mk': _L0_attn_in['Mk'], 'L0_attn_Mv': _L0_attn_in['Mv'], 'L0_ffn_sg': _L0_ffn_in['sg'], 'L0_ffn_su': _L0_ffn_in['su'], 'L0_ffn_sd': _L0_ffn_in['sd'], 'L0_ffn_rg': _L0_ffn_in['rg'], 'L0_ffn_ru': _L0_ffn_in['ru'], 'L0_ffn_rd': _L0_ffn_in['rd'], 'L0_ffn_wr': _L0_ffn_in['wr'], 'L0_ffn_rb': _L0_ffn_in['rb']}

def reference(x, cls_tok, L0_tok_cls_token, L0_tok_cls_pos_embedding, L0_tok_ln1_g, L0_tok_ln1_b, L0_tok_W, L0_tok_bias, L0_tok_ln2_g, L0_tok_ln2_b, L0_attn_Mq, L0_attn_Mk, L0_attn_Mv, L0_ffn_sg, L0_ffn_su, L0_ffn_sd, L0_ffn_rg, L0_ffn_ru, L0_ffn_rd, L0_ffn_wr, L0_ffn_rb):
    import jax
    import jax.numpy as jnp

    def _L0_tok_ref(img, cls_token, cls_pos_embedding, ln1_g, ln1_b, W, bias, ln2_g, ln2_b):
        import jax, jax.numpy as jnp
        import numpy as np
        DIM = 256
        IMG = 96
        P = 16
        C = 3
        TEMP = 10000.0
        EPS = 1e-05
        PATCH_DIM = C * P * P
        HP = IMG // P

        def layernorm(x, gamma, beta):
            mu = jnp.mean(x, axis=-1, keepdims=True)
            var = jnp.var(x, axis=-1, keepdims=True)
            return (x - mu) * jax.lax.rsqrt(var + EPS) * gamma + beta

        def posemb_sincos_2d(h, w, dim, dtype):
            y, x = jnp.meshgrid(jnp.arange(h), jnp.arange(w), indexing='ij')
            omega = jnp.arange(dim // 4, dtype=jnp.float32) / (dim // 4 - 1)
            omega = 1.0 / TEMP ** omega
            y = y.reshape(-1)[:, None] * omega[None, :]
            x = x.reshape(-1)[:, None] * omega[None, :]
            pe = jnp.concatenate((jnp.sin(x), jnp.cos(x), jnp.sin(y), jnp.cos(y)), axis=1)
            return pe.astype(dtype)
        b = img.shape[0]
        x = img.reshape(b, C, HP, P, HP, P)
        x = jnp.transpose(x, (0, 2, 4, 3, 5, 1))
        x = x.reshape(b, HP, HP, PATCH_DIM)
        x = layernorm(x, ln1_g, ln1_b)
        x = jnp.einsum('bhwp,pd->bhwd', x, W) + bias
        x = layernorm(x, ln2_g, ln2_b)
        pe = posemb_sincos_2d(HP, HP, DIM, x.dtype)
        x = x.reshape(b, HP * HP, DIM) + pe[None]
        cls_tokens = jnp.broadcast_to(cls_token + cls_pos_embedding, (b, 1, DIM))
        return jnp.concatenate((cls_tokens, x), axis=1)

    def _L0_attn_ref(x, Mq, Mk, Mv):
        import jax, jax.numpy as jnp
        import numpy as np
        HEADS = 8
        K_SIZE = 64
        B, C, _ = x.shape
        H, K = (HEADS, K_SIZE)
        V = Mv.shape[1] // H
        q = (x @ Mq).reshape(B, H, C, K)
        k = (x @ Mk).reshape(B, H, C, K)
        v = (x @ Mv).reshape(B, H, C, V)
        scores = jnp.einsum('bhqk,bhck->bhqc', q, k).reshape(B * H, C, C)
        att = jax.nn.softmax(scores / jnp.sqrt(jnp.float32(K)), axis=1)
        att4 = att.reshape(B, C, H, C)
        out = jnp.einsum('bqhc,bhcd->bqhd', att4, v)
        return out.reshape(B, C, H * V)

    def _L0_ffn_ref(x, sg, su, sd, rg, ru, rd, wr, rb):
        import jax, jax.numpy as jnp
        import numpy as np
        H, I, E_ROUTED, TOP_K = (256, 704, 7, 2)
        B, S = (4, 512)

        def _expert(h, g, u, d):
            return jnp.einsum('...i,hi->...h', jax.nn.silu(h @ g.T) * (h @ u.T), d)
        shared_out = _expert(x, sg, su, sd)
        logits = x @ wr.T + rb
        probs = jax.nn.softmax(logits, axis=-1)
        scores, idx = jax.lax.top_k(probs, TOP_K)
        scores = scores / scores.sum(axis=-1, keepdims=True)
        w = jnp.sum(scores[..., None] * jax.nn.one_hot(idx, E_ROUTED, dtype=x.dtype), axis=-2)
        out = shared_out
        for e in range(E_ROUTED):
            out = out + w[..., e:e + 1] * _expert(x, rg[e], ru[e], rd[e])
        return out
    h = _L0_tok_ref(x, L0_tok_cls_token, L0_tok_cls_pos_embedding, L0_tok_ln1_g, L0_tok_ln1_b, L0_tok_W, L0_tok_bias, L0_tok_ln2_g, L0_tok_ln2_b)
    h = jnp.concatenate([jnp.broadcast_to(cls_tok, (h.shape[0], 1, h.shape[2])), h], axis=1)
    h = h + _L0_attn_ref(_layernorm(h, axis=-1), L0_attn_Mq, L0_attn_Mk, L0_attn_Mv)
    h = h + _L0_ffn_ref(_layernorm(h, axis=-1), L0_ffn_sg, L0_ffn_su, L0_ffn_sd, L0_ffn_rg, L0_ffn_ru, L0_ffn_rd, L0_ffn_wr, L0_ffn_rb)
    return h

_drawn_inputs = setup_inputs


def setup_inputs(seed=0):
    import zlib

    import numpy as np

    out = dict(_drawn_inputs(seed))
    spreads = {'L0_tok_ln1_g': (1.0, 0.2),
     'L0_tok_ln1_b': (0.0, 0.1),
     'L0_tok_bias': (0.0, 0.1),
     'L0_tok_ln2_g': (1.0, 0.2),
     'L0_tok_ln2_b': (0.0, 0.1),
     'L0_ffn_rb': (0.0, 0.8)}
    factors = {'cls_tok': 7.611,
     'L0_attn_Mq': 8.0,
     'L0_attn_Mk': 8.0,
     'L0_ffn_rg': 3.602,
     'L0_ffn_ru': 3.572,
     'L0_ffn_rd': 3.572,
     'L0_ffn_wr': 4.221}
    for name, (base, spread) in spreads.items():
        noise = np.random.default_rng([zlib.crc32(name.encode()), seed]).standard_normal(out[name].shape)
        drawn = base * np.exp(spread * noise) if base else spread * noise
        out[name] = jnp.asarray(drawn.astype(out[name].dtype))
    for name, factor in factors.items():
        out[name] = (out[name] * factor).astype(out[name].dtype)
    return out
```

```python
from contextlib import ExitStack

import numpy as np

import concourse.bass as bass
from concourse import mybir
from concourse.alu_op_type import AluOpType as ALU

F32, F16, I32, U32 = mybir.dt.float32, mybir.dt.float16, mybir.dt.int32, mybir.dt.uint32
ACT = mybir.ActivationFunctionType
X = mybir.AxisListType.X

P = 128
IMAGES, SIDE, PATCH, CHANNELS = 64, 96, 16, 3
GRID = SIDE // PATCH
TOKENS = GRID * GRID + 2
PIXELS = CHANNELS * PATCH * PATCH
PIX_BLOCKS = PIXELS // P
DIM = 256
DIM_BLOCKS = DIM // P
PICKED = GRID * GRID + 4
ROWS = IMAGES * TOKENS
TILES = ROWS // P
EPS = 1e-5

HEADS, KEY, VAL = 8, 64, 32
QK = HEADS * KEY
CHUNK_IMAGES = 8
CHUNKS = IMAGES // CHUNK_IMAGES
CHUNK = CHUNK_IMAGES * TOKENS
CHUNK_PAIRS = CHUNK_IMAGES // 2
ROW64 = CHUNK * HEADS
IMAGE64 = TOKENS * HEADS
PAD64 = KEY - TOKENS

INNER = 704
ROUTED, TOP = 7, 2
EXPERTS = ROUTED + 1
FFN_TILE = 256
PIECE = 1536
PIECES = 3 * EXPERTS
EARLY_PIECES = 2 * CHUNKS
SLOT_TILES = (TOP * ROWS + ROUTED * (FFN_TILE - 1)) // FFN_TILE
SLOTS = SLOT_TILES * FFN_TILE

NEVER = -3e38
TAKEN = -1e30
LATE_FIRST = EARLY_PIECES

SHARED_EARLY = 6
SHARED_LATE = ROWS // FFN_TILE - SHARED_EARLY
PHASES = (("shared", SHARED_EARLY, FFN_TILE), ("routed", SLOT_TILES, FFN_TILE),
          ("shared", SHARED_LATE, FFN_TILE), ("shared", 1, ROWS % FFN_TILE))
STARTS = [sum(p[1] for p in PHASES[:n]) for n in range(len(PHASES))]
FIRST_TOKEN = [0, 0, SHARED_EARLY * FFN_TILE, (SHARED_EARLY + SHARED_LATE) * FFN_TILE]
GATES = (0, 512, 1024)
UPS = (256, 768, 1280)

ALL_TILES = sum(p[1] for p in PHASES)
LATE_AT = {2: (16, 17), 3: (18, 19), 5: (20, 21, 22, 23)}

W_SCALE = 64.0
H_SCALE = 4.0


class Tile:

    def __init__(self, base, at, start, reuses, peeled):
        double, single = base
        self.n, self.turn, self.slot = double + at, single + at // 2, at % 2
        self.k, self.k_turn = double + (at - start), single + (at - start) // 2
        self.reuses = reuses
        self.step = at - start if peeled else None
        self.first = peeled and at == 0


def pipeline(engine, count, stages, start=0, straight=False):
    deepest = max(lag for lag, _ in stages)
    head = count if straight else min(deepest + 2, count)
    pairs = (count - head) // 2

    def peeled(step):
        for lag, stage in stages:
            if 0 <= step - lag < count:
                stage(Tile((0, 0), start + step - lag, start, step - lag >= 2, True))

    for step in range(head):
        peeled(step)
    if pairs > 0:
        with engine.Fori(0, pairs) as i:
            for step in (head, head + 1):
                for lag, stage in stages:
                    stage(Tile((2 * i, i), start + step - lag, start, True, False))
    for step in range(head + 2 * max(pairs, 0), count + deepest):
        peeled(step)


def program(nc, a, out):
    ctx = ExitStack()

    base = (nc.sbuf_base + 31) // 32 * 32
    top = base

    def place(at, name, shape, dtype):
        size = int(np.prod(shape[1:])) * mybir.dt.size(dtype)
        return nc.alloc_sbuf_tensor_at(name, shape, dtype, offset=at), (at + size + 31) // 32 * 32

    def region(at, wanted):
        placed = []
        for name, shape, dtype in wanted:
            t, at = place(at, name, shape, dtype)
            placed.append(t)
        assert at <= nc.sbuf_usable_end, (at, nc.sbuf_usable_end)
        return placed, at

    (w,), top = region(base, [("expert_w", [P, PIECES, 2, PIECE], F16)])
    late_w = base + EARLY_PIECES * 2 * PIECE * 2
    (ident, w_stage), top = region(top, [("ident", [P, P], F32), ("w_stage", [P, 2, PIECE], F32)])
    (xnT,), front = region(top, [("xnT", [P, 2, DIM_BLOCKS, ROWS], F16)])
    (mqk, mv), front = region(front, [
        ("mqk", [P, 2, DIM_BLOCKS, 2 * QK], F16), ("mv", [P, 2, DIM_BLOCKS, DIM], F16)])
    (wtok, wtok32, wtok_g, m32, pix, z, zT), used = region(base, [
        ("wtok", [P, 2, PIX_BLOCKS, DIM], F16), ("wtok32", [P, PIX_BLOCKS, DIM], F32),
        ("wtok_g", [P, PIX_BLOCKS, DIM], F32),
        ("m32", [P, DIM_BLOCKS, DIM], F32),
        ("pix", [P, 2, PIXELS], F32), ("z", [P, 2, PIXELS], F32), ("zT", [P, 2, 2, PIXELS], F16)])
    (y, y2, y2g, h0, xn0, v0, rows40, rows_hl, pick40, g1, b1, b1wide, bias_row, g2_row, is_patch,
     st1, mv1, sd1, r1, nb1, st2, mv2, sd2, r2, r2m, nb2, st3, mv3, sd3, r3, nb3), used = region(used, [
        ("y", [P, 2, DIM], F32), ("y2", [P, 2, DIM], F32), ("y2g", [P, 2, DIM], F32),
        ("h0", [P, 2, DIM], F32), ("xn0", [P, 2, DIM], F32), ("v0", [P, 2, DIM], F32),
        ("rows40", [PICKED, DIM], F32), ("rows_hl", [PICKED, 2, DIM], F16), ("pick40", [PICKED, ROWS], F16),
        ("g1", [P, PIX_BLOCKS], F32), ("b1", [P, PIX_BLOCKS], F32), ("b1wide", [P, PIX_BLOCKS, P], F32),
        ("bias_row", [P, DIM], F32), ("g2_row", [P, DIM], F32), ("is_patch", [P, TILES], F32),
        ("st1", [P, 2, 12], F32), ("mv1", [P, 2, 2], F32), ("sd1", [P, 2, 1], F32), ("r1", [P, 2, 1], F32), ("nb1", [P, 2, 1], F32),
        ("st2", [P, 2, 6], F32), ("mv2", [P, 2, 2], F32), ("sd2", [P, 2, 1], F32), ("r2", [P, 2, 1], F32), ("r2m", [P, 2, 1], F32), ("nb2", [P, 2, 1], F32),
        ("st3", [P, 2, 6], F32), ("mv3", [P, 2, 2], F32), ("sd3", [P, 2, 1], F32), ("r3", [P, 2, 1], F32), ("nb3", [P, 2, 1], F32)])
    assert used <= base + PIECES * 2 * PIECE * 2


    (q64, k64, prob), used = region(late_w, [
        ("q64", [KEY, 2, ROW64], F32), ("k64", [KEY, 2, ROW64 + 32], F32),
        ("prob", [P, 2, 2, IMAGE64], F32)])
    assert used <= base + PIECES * 2 * PIECE * 2, used
    (ob,), used = region(used, [("ob", [TOKENS, 2, 2, DIM], F32)])
    assert used <= base + PIECES * 2 * PIECE * 2, used
    (vbd, zero_row, most, total, share), used = region(front, [
        ("vbd", [P, 2, CHUNK_IMAGES // 2, HEADS, 2, VAL], F32), ("zero_row", [P, DIM], F32),
        ("most", [P, 2, 2 * HEADS], F32), ("total", [P, 2, 2 * HEADS], F32), ("share", [P, 2, 2 * HEADS], F32)])

    small_end = base + (LATE_FIRST + 4) * 2 * PIECE * 2
    (h0t, attn_t, h1t, xn4, st4, mv4, sd4, r4, nb4, logit, logit2, hit, code, first_hot, second_hot, gap, growth,
     both_hot, where, slt, ones, rev, wr32, wr_hl, rb_row, cnt, cnt_i, tiles_f, cum_a, cum_b, start_row,
     best, best_code, second, second_code, chosen), used = region(late_w, [
        ("h0t", [P, 2, DIM], F32), ("attn_t", [P, 2, DIM], F32), ("h1t", [P, 2, DIM], F32),
        ("xn4", [P, 2, DIM], F32),
        ("st4", [P, 2, 6], F32), ("mv4", [P, 2, 2], F32), ("sd4", [P, 2, 1], F32), ("r4", [P, 2, 1], F32),
        ("nb4", [P, 2, 1], F32),
        ("logit", [P, TILES, EXPERTS], F32), ("logit2", [P, TILES, EXPERTS], F32),
        ("hit", [P, TILES, EXPERTS], F32), ("code", [P, TILES, EXPERTS], F32),
        ("first_hot", [P, TILES, EXPERTS], F32), ("second_hot", [P, TILES, EXPERTS], F32),
        ("gap", [P, TILES], F32), ("growth", [P, TILES], F32),
        ("both_hot", [P, TILES, EXPERTS], F16), ("where", [P, TILES, EXPERTS], F32),
        ("slt", [P, P], F16), ("ones", [P, P], F16), ("rev", [P, EXPERTS], F32),
        ("wr32", [P, DIM_BLOCKS, EXPERTS], F32), ("wr_hl", [P, 2, DIM_BLOCKS, EXPERTS], F16),
        ("rb_row", [P, EXPERTS], F32), ("cnt", [P, EXPERTS], F32), ("cnt_i", [P, 2, EXPERTS], I32),
        ("tiles_f", [P, EXPERTS], F32), ("cum_a", [P, EXPERTS], F32), ("cum_b", [P, EXPERTS], F32),
        ("start_row", [P, EXPERTS], F32),
        ("best", [P, TILES], F32), ("best_code", [P, TILES], F32),
        ("second", [P, TILES], F32), ("second_code", [P, TILES], F32), ("chosen", [P, 2, TILES], F32)])
    assert used <= small_end, (used, small_end)
    (xn_all,), used = region(small_end, [("xn_all", [P, TILES, DIM], F32)])
    assert used <= base + PIECES * 2 * PIECE * 2
    (xTs, xg, xh, silu, prod, hT, yo, weight, pos, bounds), used = region(top, [
        ("xTs", [P, 2, DIM_BLOCKS, ROWS], F16),
        ("xg", [P, 2, 2, DIM], F32),
        ("xh", [P, 2, 2, DIM_BLOCKS, FFN_TILE], F16),
        ("silu", [P, 2, 2 * FFN_TILE], F32), ("prod", [P, 2, 2 * FFN_TILE], F32),
        ("hT", [P, 2, 2, 6, FFN_TILE], F16),
        ("yo", [P, 2, 2, DIM], F32),
        ("weight", [P, TOP, TILES], F32), ("pos", [P, TOP, TILES], I32), ("bounds", [P, EXPERTS], I32)])
    (picked, base_t, mixed), _ = region(base + PIECES * 2 * PIECE * 2 + P * 4, [
        ("picked", [P, 2, TOP, DIM], F32), ("base_t", [P, 2, DIM], F32), ("mixed", [P, 2, DIM], F32)])

    mqk32 = w_stage[:].rearrange("p s x -> p (s x)")[:, 0:DIM_BLOCKS * 2 * QK].rearrange("p (b x) -> p b x", b=DIM_BLOCKS)

    banks = ctx.enter_context(nc.psum_tensor("banks", [P, 8, 512], F32))

    def dram(name, shape, dtype=F32):
        t = nc.dram_tensor(name, shape, dtype, kind="Internal")
        return t.ap()

    h0_d = dram("h0_d", (ROWS, DIM))
    v_d = dram("v_d", (ROWS, DIM))

    attn_d = dram("attn_d", (ROWS, DIM))
    h1_d = dram("h1_d", (ROWS, DIM))
    xslot_d = dram("xslot_d", (SLOTS, DIM))
    yslot_d = dram("yslot_d", (SLOTS, DIM))
    shared_d = dram("shared_d", (ROWS, DIM))

    def sem(name):
        return ctx.enter_context(nc.semaphore(name))

    consts_loaded = sem("consts_loaded")
    wtok_loaded, m_loaded = sem("wtok_loaded"), sem("m_loaded")
    ident_ready = sem("ident_ready")
    pix_loaded = [sem(f"pix_loaded{s}") for s in range(2)]
    wtok_scaled, wtok_hi, wtok_ready, bias_made, b1_wide, bias_ready = (
        sem(n) for n in ("wtok_scaled", "wtok_hi", "wtok_ready", "bias_made", "b1_wide", "bias_ready"))
    rows_hi, rows_ready = sem("rows_hi"), sem("rows_ready")
    m_hi, m_ready = sem("m_hi"), sem("m_ready")
    mqk_loaded = [sem(f"mqk_loaded{s}") for s in range(2)]
    aggr1, std1, rcp1, shift1, z_ready = (
        sem(n) for n in ("aggr1", "std1", "rcp1", "shift1", "z_ready"))
    zT_made, zT_hi, zT_ready, y_made, y_ready = (
        sem(n) for n in ("zT_made", "zT_hi", "zT_ready", "y_made", "y_ready"))
    aggr2, std2, rcp2, mask2, shift2, y2_ready, y2g_ready, h0_ready = (
        sem(n) for n in ("aggr2", "std2", "rcp2", "mask2", "shift2", "y2_ready", "y2g_ready", "h0_ready"))
    aggr3, std3, rcp3, shift3, xn0_ready, xT_made, xT_hi, xT_ready, v_made, v_ready = (
        sem(n) for n in ("aggr3", "std3", "rcp3", "shift3", "xn0_ready", "xT_made", "xT_hi", "xT_ready", "v_made", "v_ready"))
    h0_stored = [sem(f"h0_stored{s}") for s in range(2)]
    v_stored = [sem(f"v_stored{s}") for s in range(2)]

    m_qk_loaded, m_qk_hi, m_qk_ready, vbd_zero, pad_zero = (
        sem(n) for n in ("m_qk_loaded", "m_qk_hi", "m_qk_ready", "vbd_zero", "pad_zero"))
    piece_loaded = [sem(f"piece_loaded{s}") for s in range(2)]
    piece_hi, piece_ready = sem("piece_hi"), sem("piece_ready")
    vbd_loaded = [sem(f"vbd_loaded{s}") for s in range(2)]
    proj_made, proj_even, proj_odd = sem("proj_made"), sem("proj_even"), sem("proj_odd")
    score_begun, score_made, most_ready, centred, exp_ready, total_ready, share_ready, prob_ready = (
        sem(n) for n in ("score_begun", "score_made", "most_ready", "centred", "exp_ready", "total_ready", "share_ready", "prob_ready"))
    o_made, o_ready = sem("o_made"), sem("o_ready")
    o_stored = [sem(f"o_stored{s}") for s in range(2)]

    row_zero, slots_zero = sem("row_zero"), sem("slots_zero")
    route_loaded, h0t_loaded = sem("route_loaded"), [sem(f"h0t_loaded{s}") for s in range(2)]
    xn_kept = [sem(f"xn_kept{s}") for s in range(2)]
    h1_stored = [sem(f"h1_stored{s}") for s in range(2)]
    router_hi, router_ready, h1_ready, aggr4, std4, rcp4, shift4, xn_ready = (
        sem(n) for n in ("router_hi", "router_ready", "h1_ready", "aggr4", "std4", "rcp4", "shift4", "xn_ready"))
    x4_made, x4_hi, x4_ready, logit_made, logit_ready = (
        sem(n) for n in ("x4_made", "x4_hi", "x4_ready", "logit_made", "logit_ready"))
    routed_step, gap_ready, growth_ready, hot_ready, rank_made, weight_ready, pos_ready = (
        sem(n) for n in ("routed_step", "gap_ready", "growth_ready", "hot_ready", "rank_made", "weight_ready", "pos_ready"))
    scattered = sem("scattered")
    xg_loaded = [[sem(f"xg_loaded{p}_{s}") for s in range(2)] for p in range(len(PHASES))]
    late_loaded = [sem(f"late_loaded{s}") for s in range(2)]
    late_hi, late_ready, prod_zero = sem("late_hi"), sem("late_ready"), sem("prod_zero")
    xT4_made, xh_hi, xh_ready = sem("xT4_made"), sem("xh_hi"), sem("xh_ready")
    gu_made, silu_ready, prod_ready, hT_hi, hT_ready, down_made, y_out = (
        sem(n) for n in ("gu_made", "silu_ready", "prod_ready", "hT_hi", "hT_ready", "down_made", "y_out"))
    y_stored = [sem(f"y_stored{s}") for s in range(2)]
    gathered = [sem(f"gathered{s}") for s in range(2)]
    base_loaded = [sem(f"base_loaded{s}") for s in range(2)]
    half_mixed, mixed_ready = sem("half_mixed"), sem("mixed_ready")
    out_stored = [sem(f"out_stored{s}") for s in range(2)]

    def stored_counts(sems, count, each=16):
        return [(sems[s], each * ((count + 1 - s) // 2)) for s in range(2)]

    def rows_of(dram_ap, t, n=P):
        return dram_ap[bass.ds(t * n, n), :]

    def tokens_of(t, n=P):
        return bass.ds(t * n, n)

    def row64(c, b, half):
        side = q64 if b < 4 else k64
        return side[:, c.slot, 0:ROW64].rearrange("k (t g) -> k t g", g=HEADS)[:, :, 2 * (b % 4) + half]

    def by_head(scores):
        return scores.rearrange("p b (h q) -> p (b h) q", q=TOKENS)

    def by_bank_head(scores):
        return scores.rearrange("p b (h q) -> p b h q", q=TOKENS)

    def scores_of(g):
        return banks[:, 2 + 2 * g:4 + 2 * g, 0:IMAGE64]

    THIRD = PIX_BLOCKS // 2

    block = ctx.enter_context(nc.Block())

    @block.sync
    def _(sp):
        sp.dma_start(wtok32[:], a["w_tok"]).then_inc(wtok_loaded, 16)
        sp.dma_start(g1[:], a["ln1_g"]).then_inc(wtok_loaded, 16)

        def load_pixels(t):
            if t.reuses:
                sp.wait_ge(z_ready, t.n - 1)
            sp.dma_start(pix[:, t.slot, :], a["patches"][bass.ds(t.n, 1)].rearrange("o p x -> (o p) x")).then_inc(pix_loaded[t.slot], 16)

        def store_tokens(t):
            sp.wait_ge(h0_ready, t.n + 1)
            sp.dma_start(rows_of(h0_d, t.n), h0[:, t.slot, :]).then_inc(h0_stored[t.slot], 16)

        def store_values(t):
            sp.wait_ge(v_ready, t.n + 1)
            sp.dma_start(rows_of(v_d, t.n), v0[:, t.slot, :]).then_inc(v_stored[t.slot], 16)

        first = [True]

        def load_rest(t):
            if t.first:
                for dst, name in ((b1, "ln1_b"), (bias_row, "tok_bias"), (g2_row, "ln2_g"),
                                  (is_patch, "is_patch"), (rows40, "rows40"), (pick40, "pick40")):
                    src = a[name]
                    if name in ("tok_bias", "ln2_g"):
                        src = src.partition_broadcast(P)
                    sp.dma_start(dst[:], src).then_inc(consts_loaded, 16)
                sp.dma_start(m32[:], a["Mv"]).then_inc(m_loaded, 16)
                sp.dma_start(mqk32, a["Mqk"]).then_inc(m_qk_loaded, 16)

        pipeline(sp, TILES, [(0, load_pixels), (0, load_rest), (3, store_tokens), (5, store_values)])
        for stored, count in stored_counts(h0_stored, TILES) + stored_counts(v_stored, TILES):
            sp.wait_ge(stored, count)

        def load_values(c):
            if c.first:
                sp.wait_ge(vbd_zero, 1)
            if c.reuses:
                sp.wait_ge(o_made, 4 * (c.n - 1))
            for pair in range(CHUNK_IMAGES // 2):
                for b in range(2):
                    image = v_d[bass.ds(c.n * CHUNK + (2 * pair + b) * TOKENS, TOKENS), :]
                    sp.dma_start(vbd[64 * b:64 * b + TOKENS, c.slot, pair, :, b, :],
                                 image.rearrange("t (g d) -> (t g) d", d=VAL).rearrange("(h k) d -> k h d", k=TOKENS)
                                 ).then_inc(vbd_loaded[c.slot], 16)

        def load_pieces(c):
            for s in range(2):
                if not c.first:
                    sp.wait_ge(piece_ready, 2 * c.n + s - 1)
                else:
                    sp.wait_ge(m_qk_ready, 1)
                sp.dma_start(w_stage[:, s], piece_of(2 * c.n + s)).then_inc(piece_loaded[s], 16)

        def piece_of(n):
            return a["pieces"][bass.ds(n, 1)].rearrange("o p x -> (o p) x")

        def store_attention(c):
            for pair in range(CHUNK_IMAGES // 2):
                sp.wait_ge(o_ready, 4 * c.n + pair + 1)
                sp.dma_start(attn_d[bass.ds(c.n * CHUNK + 2 * pair * TOKENS, 2 * TOKENS), :]
                             .rearrange("(b q) d -> q b d", b=2),
                             ob[:, pair % 2]).then_inc(o_stored[pair % 2], 16)

        pipeline(sp, CHUNKS, [(0, load_values), (0, load_pieces), (1, store_attention)])
        for s in range(2):
            sp.wait_ge(o_stored[s], 16 * 2 * CHUNKS)

        def load_residual(t):
            if t.reuses:
                sp.wait_ge(h1_ready, t.n - 1)
            sp.dma_start(h0t[:, t.slot], rows_of(h0_d, t.n)).then_inc(h0t_loaded[t.slot], 16)
            sp.dma_start(attn_t[:, t.slot], rows_of(attn_d, t.n)).then_inc(h0t_loaded[t.slot], 16)

        def store_h1(t):
            sp.wait_ge(h1_ready, t.n + 1)
            sp.dma_start(rows_of(h1_d, t.n), h1t[:, t.slot]).then_inc(h1_stored[t.slot], 16)

        def keep_normalised(t):
            sp.wait_ge(xn_ready, t.n + 1)
            sp.dma_start(xn_all[:, bass.ds(t.n, 1)].rearrange("p o d -> p (o d)"), xn4[:, t.slot]).then_inc(xn_kept[t.slot], 16)

        sp.wait_ge(o_made, 4 * CHUNKS)
        for dst, src in ((wr32, a["router"]), (rb_row, a["router_bias"].partition_broadcast(P)),
                         (rev, a["rev"].partition_broadcast(P)), (slt, a["slt"]), (ones, a["ones"])):
            sp.dma_start(dst[:], src).then_inc(route_loaded, 16)
        pipeline(sp, TILES, [(0, load_residual), (1, store_h1), (2, keep_normalised)])
        for stored, count in stored_counts(h1_stored, TILES):
            sp.wait_ge(stored, count)

        def tile_rows(phase, t):
            kind, _, width = PHASES[phase]
            return bass.ds(t.k * width + FIRST_TOKEN[phase], width)

        def load_input(phase):
            source = xslot_d if PHASES[phase][0] == "routed" else h1_d
            halves = PHASES[phase][2] // P

            def stage(t):
                if t.step is None or t.n >= 2:
                    sp.wait_ge(y_out, t.n - 1)
                sp.dma_start(xg[:, t.slot, 0:halves], source[tile_rows(phase, t), :].rearrange("(s p) d -> p s d", p=P)
                             ).then_inc(xg_loaded[phase][t.slot], 16)
            return stage

        def store_result(phase):
            target = yslot_d if PHASES[phase][0] == "routed" else shared_d
            halves = PHASES[phase][2] // P

            def stage(t):
                sp.wait_ge(y_out, t.n + 1)
                sp.dma_start(target[tile_rows(phase, t), :].rearrange("(s p) d -> p s d", p=P), yo[:, t.slot, 0:halves]
                             ).then_inc(y_stored[t.slot], 16)
            return stage

        def load_late_pieces(t):
            for n in LATE_AT.get(t.step, ()):
                late = n - LATE_FIRST
                if late >= 2:
                    sp.wait_ge(late_ready, late - 1)
                sp.dma_start(w_stage[:, late % 2], a["pieces"][n]).then_inc(late_loaded[late % 2], 16)

        for phase, (kind, count, _) in enumerate(PHASES):
            if kind == "routed":
                sp.wait_ge(scattered, 16 * TOP * TILES)
            early = [(0, load_late_pieces)] if phase == 0 else []
            pipeline(sp, count, [(0, load_input(phase))] + early + [(2, store_result(phase))], STARTS[phase], phase == 0)
            if phase == 1:
                sp.wait_ge(late_ready, PIECES - LATE_FIRST)
        for stored, count in stored_counts(y_stored, ALL_TILES):
            sp.wait_ge(stored, count)
        for t in range(TILES):
            if t >= 2:
                sp.wait_ge(half_mixed, t - 1)
            sp.dma_start(base_t[:, t % 2], rows_of(shared_d, t)).then_inc(base_loaded[t % 2], 16)
            if t:
                sp.wait_ge(mixed_ready, t)
                sp.dma_start(rows_of(out, t - 1), mixed[:, (t - 1) % 2]).then_inc(out_stored[(t - 1) % 2], 16)
        sp.wait_ge(mixed_ready, TILES)
        sp.dma_start(rows_of(out, TILES - 1), mixed[:, (TILES - 1) % 2]).then_inc(out_stored[(TILES - 1) % 2], 16)
        for stored, count in stored_counts(out_stored, TILES):
            sp.wait_ge(stored, count)

    @block.gpsimd
    def _(pool):
        nc.gpsimd.memset(ident[:], 0.0).then_inc(ident_ready, 1)
        pool.wait_ge(ident_ready, 1)
        nc.gpsimd.affine_select(out=ident[:], in_=ident[:], compare_op=ALU.not_equal, fill=1.0, base=0,
                                pattern=[[-1, P]], channel_multiplier=1).then_inc(ident_ready, 1)
        nc.gpsimd.memset(vbd[:], 0.0).then_inc(vbd_zero, 1)
        nc.gpsimd.memset(k64[:, :, ROW64:], 0.0).then_inc(pad_zero, 1)
        nc.gpsimd.memset(zero_row[:], 0.0).then_inc(row_zero, 1)
        pool.wait_ge(consts_loaded, 16 * 6)
        nc.gpsimd.tensor_copy(b1wide[:], b1[:].unsqueeze(2).to_broadcast([P, PIX_BLOCKS, P])).then_inc(b1_wide, 1)

        def gain(t):
            pool.wait_ge(y2_ready, t.n + 1)
            if t.reuses:
                pool.wait_ge(h0_ready, t.n - 1)
            nc.gpsimd.tensor_tensor(y2g[:, t.slot, :], y2[:, t.slot, :], g2_row[:], ALU.mult).then_inc(y2g_ready, 1)

        pipeline(pool, TILES, [(2, gain)])

        def shares(c):
            for g in range(2):
                pool.wait_ge(share_ready, 2 * c.n + g + 1)
                nc.gpsimd.tensor_tensor(by_head(prob[:, g]), by_head(prob[:, g]),
                                        share[:, g].unsqueeze(2).to_broadcast([P, 2 * HEADS, TOKENS]), ALU.mult
                                        ).then_inc(prob_ready, 1)

        pool.wait_ge(row_zero, 1)
        pool.dma_start(xslot_d.rearrange("(n p) d -> p n d", p=P),
                       zero_row[:].unsqueeze(1).to_broadcast([P, SLOTS // P, DIM])).then_inc(slots_zero, 16)
        pipeline(pool, CHUNKS, [(1, shares)])

        pool.wait_ge(x4_ready, TILES)
        pool.wait_ge(slots_zero, 16)
        nc.gpsimd.memset(prod[:], 0.0).then_inc(prod_zero, 1)
        for kept, count in stored_counts(xn_kept, TILES):
            pool.wait_ge(kept, count)
        pool.wait_ge(pos_ready, 1)
        for t in range(TILES):
            for choice in range(TOP):
                pool.indirect_dma_start(xslot_d[:], bass.IndirectOffsetOnAxis(ap=pos[:, choice, t:t + 1], axis=0),
                                        xn_all[:, t], None).then_inc(scattered, 16)
        pool.wait_ge(late_ready, PIECES - LATE_FIRST)
        for stored, count in stored_counts(y_stored, STARTS[2]):
            pool.wait_ge(stored, count)
        for t in range(TILES):
            if t >= 2:
                pool.wait_ge(mixed_ready, t - 1)
            for choice in range(TOP):
                pool.indirect_dma_start(picked[:, t % 2, choice], None, yslot_d[:],
                                        bass.IndirectOffsetOnAxis(ap=pos[:, choice, t:t + 1], axis=0)
                                        ).then_inc(gathered[t % 2], 16)

    @block.scalar
    def _(act):
        nc.scalar.preload_act_table(ACT.Sqrt)
        act.wait_ge(wtok_scaled, PIX_BLOCKS)
        nc.scalar.activation(wtok[:, 0], wtok_g[:], ACT.Copy).then_inc(wtok_hi, 1)
        act.wait_ge(consts_loaded, 16 * 6)
        nc.scalar.activation(rows_hl[:, 0], rows40[:], ACT.Copy).then_inc(rows_hi, 1)

        def v_weights(t):
            if t.first:
                act.wait_ge(m_loaded, 16)
                nc.scalar.activation(mv[:, 0], m32[:], ACT.Copy, scale=W_SCALE).then_inc(m_hi, 1)
                act.wait_ge(m_qk_loaded, 16)
                nc.scalar.activation(mqk[:, 0], mqk32, ACT.Copy, scale=W_SCALE).then_inc(m_qk_hi, 1)

        def split_zT(t):
            for half in range(2):
                cols = slice(half * 384, half * 384 + 384)
                act.wait_ge(zT_made, 2 * t.n + half + 1)
                if t.reuses and half == 0:
                    act.wait_ge(y_made, t.n - 1)
                nc.scalar.activation(zT[:, t.slot, 0, cols], banks[:, half, 0:384], ACT.Copy).then_inc(zT_hi, 1)

        def sqrt1(t):
            act.wait_ge(aggr1, t.n + 1)
            nc.scalar.activation(sd1[:, t.slot], mv1[:, t.slot, 1:2], ACT.Sqrt, bias=EPS).then_inc(std1, 1)

        def sqrt2(t):
            act.wait_ge(aggr2, t.n + 1)
            nc.scalar.activation(sd2[:, t.slot], mv2[:, t.slot, 1:2], ACT.Sqrt, bias=EPS).then_inc(std2, 1)

        def sqrt3(t):
            act.wait_ge(aggr3, t.n + 1)
            nc.scalar.activation(sd3[:, t.slot], mv3[:, t.slot, 1:2], ACT.Sqrt, bias=EPS).then_inc(std3, 1)

        def norm1(t):
            act.wait_ge(shift1, t.n + 1)
            if t.reuses:
                act.wait_ge(zT_made, 2 * (t.n - 1))
            nc.scalar.activation(z[:, t.slot], pix[:, t.slot], ACT.Identity, scale=r1[:, t.slot],
                                 bias=nb1[:, t.slot]).then_inc(z_ready, 1)

        def norm2(t):
            act.wait_ge(shift2, t.n + 1)
            if t.reuses:
                act.wait_ge(y2g_ready, t.n - 1)
            nc.scalar.activation(y2[:, t.slot], y[:, t.slot], ACT.Identity, scale=r2m[:, t.slot],
                                 bias=nb2[:, t.slot]).then_inc(y2_ready, 1)

        def norm3(t):
            act.wait_ge(shift3, t.n + 1)
            if t.reuses:
                act.wait_ge(xT_made, t.n - 1)
            nc.scalar.activation(xn0[:, t.slot], h0[:, t.slot], ACT.Identity, scale=r3[:, t.slot],
                                 bias=nb3[:, t.slot]).then_inc(xn0_ready, 1)

        def split_xT(t):
            act.wait_ge(xT_made, t.n + 1)
            nc.scalar.activation(xnT[:, 0, :, tokens_of(t.n)],
                                 banks[:, 4 + t.slot, 0:DIM].rearrange("p (b n) -> p b n", b=DIM_BLOCKS),
                                 ACT.Copy).then_inc(xT_hi, 1)

        def values(t):
            act.wait_ge(v_made, t.n + 1)
            if t.reuses:
                act.wait_ge(v_stored[t.slot], 16 * t.turn)
            nc.scalar.activation(v0[:, t.slot], banks[:, 6 + t.slot, 0:DIM], ACT.Copy,
                                 scale=1 / W_SCALE).then_inc(v_ready, 1)

        pipeline(act, TILES, [(1, split_zT), (2, sqrt2), (0, sqrt1), (2, norm2), (3, split_xT), (0, norm1),
                              (2, sqrt3), (0, v_weights), (4, values), (2, norm3)])

        def even_keys(blocks):
            def stage(c):
                for b in blocks:
                    act.wait_ge(proj_made, 8 * c.n + b + 1)
                    nc.scalar.activation(row64(c, b, 0), banks[0:KEY, b % 2, 0:CHUNK], ACT.Copy,
                                         scale=1 / W_SCALE).then_inc(proj_even, 1)
            return stage

        def exps(g):
            def stage(c):
                act.wait_ge(centred, 2 * c.n + g + 1)
                nc.scalar.activation(prob[:, g], prob[:, g], ACT.Exp, scale=KEY ** -0.5).then_inc(exp_ready, 1)
            return stage

        def outputs(c):
            for pair in range(CHUNK_IMAGES // 2):
                act.wait_ge(o_made, 4 * c.n + pair + 1)
                if pair >= 2 or not c.first:
                    act.wait_ge(o_stored[pair % 2], 16 * (2 * c.n + pair // 2))
                nc.scalar.activation(ob[:, pair % 2].rearrange("q b (h d) -> q b h d", d=VAL),
                                     banks[0:TOKENS, 6 + pair % 2, :].rearrange("q (h b d) -> q b h d", b=2, d=VAL),
                                     ACT.Copy).then_inc(o_ready, 1)

        def high_pieces(c):
            for s in range(2):
                act.wait_ge(piece_loaded[s], 16 * (c.n + 1))
                nc.scalar.activation(w[:, bass.ds(2 * c.n + s, 1), 0].rearrange("p o x -> p (o x)"), w_stage[:, s],
                                     ACT.Copy, scale=W_SCALE).then_inc(piece_hi, 1)

        for stored, count in stored_counts(h0_stored, TILES) + stored_counts(v_stored, TILES):
            act.wait_ge(stored, count)
        nc.scalar.preload_act_table(ACT.Exp)
        pipeline(act, CHUNKS, [(0, even_keys((0, 1))), (1, exps(0)), (0, even_keys((2, 3))), (1, exps(1)),
                               (0, even_keys((4, 5, 6, 7))), (1, outputs), (0, high_pieces)])

        def sqrt4(t):
            act.wait_ge(aggr4, t.n + 1)
            nc.scalar.activation(sd4[:, t.slot], mv4[:, t.slot, 1:2], ACT.Sqrt, bias=EPS).then_inc(std4, 1)

        def norm4(t):
            act.wait_ge(shift4, t.n + 1)
            if t.reuses:
                act.wait_ge(x4_made, t.n - 1)
                act.wait_ge(xn_kept[t.slot], 16 * t.turn)
            nc.scalar.activation(xn4[:, t.slot], h1t[:, t.slot], ACT.Identity,
                                 scale=r4[:, t.slot], bias=nb4[:, t.slot]).then_inc(xn_ready, 1)

        def high_x4(t):
            act.wait_ge(x4_made, t.n + 1)
            nc.scalar.activation(xTs[:, 0, :, tokens_of(t.n)],
                                 banks[:, t.slot, 0:DIM].rearrange("p (b n) -> p b n", b=DIM_BLOCKS),
                                 ACT.Copy).then_inc(x4_hi, 1)

        act.wait_ge(route_loaded, 16 * 5)
        nc.scalar.activation(wr_hl[:, 0], wr32[:], ACT.Copy, scale=W_SCALE).then_inc(router_hi, 1)
        nc.scalar.preload_act_table(ACT.Sqrt)
        pipeline(act, TILES, [(0, sqrt4), (1, norm4), (2, high_x4)])
        act.wait_ge(gap_ready, 1)
        nc.scalar.preload_act_table(ACT.Exp)
        nc.scalar.activation(growth[:], gap[:], ACT.Exp).then_inc(growth_ready, 1)

        def high_xh(t):
            act.wait_ge(xT4_made, t.k + 1)
            if t.step is None or t.step >= 2:
                act.wait_ge(gu_made, 3 * (t.n - 1))
            nc.scalar.activation(xh[:, t.slot, 0].rearrange("p b n -> p (b n)"), banks[:, 0], ACT.Copy).then_inc(xh_hi, 1)

        def gates(q, width):
            def stage(t):
                step, s = 3 * t.n + q, (t.slot + q) % 2
                act.wait_ge(gu_made, step + 1)
                if t.step is None or t.n > 0 or q == 2:
                    act.wait_ge(prod_ready, step - 1)
                view = silu[:, s].rearrange("p (b n) -> p b n", b=2)[:, :, 0:width]
                nc.scalar.activation(view, banks[:, 1 + s].rearrange("p (b n) -> p b n", b=2)[:, :, 0:width],
                                     ACT.Silu, scale=1 / W_SCALE).then_inc(silu_ready, 1)
            return stage

        def high_hT(q, width):
            def stage(t):
                step, s = 3 * t.n + q, (t.slot + q) % 2
                act.wait_ge(prod_ready, step + 1)
                if q == 0 and (t.step is None or t.n >= 2):
                    act.wait_ge(down_made, t.n - 1)
                nc.scalar.activation(hT[:, t.slot, 0, 2 * q:2 * q + 2, 0:width],
                                     prod[:, s].rearrange("p (b n) -> p b n", b=2)[:, :, 0:width], ACT.Copy
                                     ).then_inc(hT_hi, 1)
            return stage

        def routed_results(t):
            act.wait_ge(down_made, t.n + 1)
            act.wait_ge(y_stored[t.slot], 16 * t.turn)
            nc.scalar.activation(yo[:, t.slot], banks[:, 5:7, 0:DIM], ACT.Copy, scale=1 / (W_SCALE * H_SCALE)
                                 ).then_inc(y_out, 1)

        def high_late_pieces(t):
            for n in LATE_AT.get(t.step, ()):
                late = n - LATE_FIRST
                act.wait_ge(late_loaded[late % 2], 16 * (late // 2 + 1))
                act.wait_ge(pos_ready, 1)
                if late >= 4:
                    act.wait_ge(scattered, 16 * TOP * TILES)
                nc.scalar.activation(w[:, n, 0], w_stage[:, late % 2], ACT.Copy, scale=W_SCALE).then_inc(late_hi, 1)

        nc.scalar.preload_act_table(ACT.Silu)
        act.wait_ge(prod_zero, 1)
        for phase, (kind, count, width) in enumerate(PHASES):
            routed = kind == "routed"
            before = [(0, high_xh)] if routed else [(0, high_late_pieces)] if phase == 0 else []
            after = [(2, routed_results)] if routed else []
            pipeline(act, count, [(1, gates(0, width)), (1, high_hT(0, width))] + after + [
                (1, gates(1, width)), (1, high_hT(1, width))] + before + [
                (1, gates(2, width)), (1, high_hT(2, width))], STARTS[phase], phase == 0)

    @block.vector
    def _(dve):
        dve.wait_ge(wtok_loaded, 32)
        for b in range(PIX_BLOCKS):
            nc.vector.tensor_scalar(wtok_g[:, b], wtok32[:, b], g1[:, b:b + 1], W_SCALE, ALU.mult, ALU.mult
                                    ).then_inc(wtok_scaled, 1)
        dve.wait_ge(wtok_hi, 1)
        nc.vector.tensor_tensor(wtok[:, 1], wtok_g[:], wtok[:, 0], ALU.subtract).then_inc(wtok_ready, 1)
        dve.wait_ge(rows_hi, 1)
        nc.vector.tensor_tensor(rows_hl[:, 1], rows40[:], rows_hl[:, 0], ALU.subtract).then_inc(rows_ready, 1)

        def stats_of_pixels(t):
            dve.wait_ge(pix_loaded[t.slot], 16 * (t.turn + 1))
            for half in range(2):
                nc.vector.bn_stats(st1[:, t.slot, 6 * half:6 * half + 6],
                                   pix[:, t.slot, 384 * half:384 * half + 384])
            dve.drain()
            nc.vector.bn_aggr(mv1[:, t.slot], st1[:, t.slot]).then_inc(aggr1, 1)

        def scale1(t):
            dve.wait_ge(std1, t.n + 1)
            nc.vector.reciprocal(r1[:, t.slot], sd1[:, t.slot]).then_inc(rcp1, 1)
            dve.wait_ge(rcp1, t.n + 1)
            nc.vector.scalar_tensor_tensor(out=nb1[:, t.slot], in0=mv1[:, t.slot, 0:1], scalar=-1.0,
                                           in1=r1[:, t.slot], op0=ALU.mult, op1=ALU.mult).then_inc(shift1, 1)

        def low_zT(half):
            def stage(t):
                cols = slice(half * 384, half * 384 + 384)
                dve.wait_ge(zT_hi, 2 * t.n + half + 1)
                nc.vector.tensor_tensor(zT[:, t.slot, 1, cols], banks[:, half, 0:384], zT[:, t.slot, 0, cols],
                                        ALU.subtract).then_inc(zT_ready, 1)
            return stage

        def v_weights(t):
            if t.first:
                dve.wait_ge(m_hi, 1)
                nc.vector.scalar_tensor_tensor(out=mv[:, 1], in0=m32[:], scalar=W_SCALE, in1=mv[:, 0],
                                               op0=ALU.mult, op1=ALU.subtract).then_inc(m_ready, 1)
                dve.wait_ge(m_qk_hi, 1)
                nc.vector.scalar_tensor_tensor(out=mqk[:, 1], in0=mqk32, scalar=W_SCALE, in1=mqk[:, 0],
                                               op0=ALU.mult, op1=ALU.subtract).then_inc(m_qk_ready, 1)
                dve.wait_ge(bias_made, 1)
                nc.vector.tensor_tensor(bias_row[:], banks[:, 7, 0:DIM], bias_row[:], ALU.add).then_inc(bias_ready, 1)
                dve.wait_ge(bias_ready, 1)

        def embed(t):
            dve.wait_ge(y_made, t.n + 1)
            if t.reuses:
                dve.wait_ge(y2_ready, t.n - 1)
            nc.vector.scalar_tensor_tensor(out=y[:, t.slot], in0=banks[:, 2 + t.slot, 0:DIM], scalar=1 / W_SCALE,
                                           in1=bias_row[:], op0=ALU.mult, op1=ALU.add).then_inc(y_ready, 1)
            dve.wait_ge(y_ready, t.n + 1)
            nc.vector.bn_stats(st2[:, t.slot], y[:, t.slot])
            dve.drain()
            nc.vector.bn_aggr(mv2[:, t.slot], st2[:, t.slot]).then_inc(aggr2, 1)

        def scale2(t):
            dve.wait_ge(std2, t.n + 1)
            nc.vector.reciprocal(r2[:, t.slot], sd2[:, t.slot]).then_inc(rcp2, 1)
            dve.wait_ge(rcp2, t.n + 1)
            nc.vector.tensor_tensor(r2m[:, t.slot], r2[:, t.slot], is_patch[:, bass.ds(t.n, 1)], ALU.mult
                                    ).then_inc(mask2, 1)
            dve.wait_ge(mask2, t.n + 1)
            nc.vector.scalar_tensor_tensor(out=nb2[:, t.slot], in0=mv2[:, t.slot, 0:1], scalar=-1.0,
                                           in1=r2m[:, t.slot], op0=ALU.mult, op1=ALU.mult).then_inc(shift2, 1)

        def tokens(t):
            dve.wait_ge(y2g_ready, t.n + 1)
            if t.reuses:
                dve.wait_ge(h0_stored[t.slot], 16 * t.turn)
                dve.wait_ge(xn0_ready, t.n - 1)
            nc.vector.tensor_tensor(h0[:, t.slot], banks[:, 2 + t.slot, DIM:2 * DIM], y2g[:, t.slot], ALU.add
                                    ).then_inc(h0_ready, 1)
            dve.wait_ge(h0_ready, t.n + 1)
            nc.vector.bn_stats(st3[:, t.slot], h0[:, t.slot])
            dve.drain()
            nc.vector.bn_aggr(mv3[:, t.slot], st3[:, t.slot]).then_inc(aggr3, 1)

        def scale3(t):
            dve.wait_ge(std3, t.n + 1)
            nc.vector.reciprocal(r3[:, t.slot], sd3[:, t.slot]).then_inc(rcp3, 1)
            dve.wait_ge(rcp3, t.n + 1)
            nc.vector.scalar_tensor_tensor(out=nb3[:, t.slot], in0=mv3[:, t.slot, 0:1], scalar=-1.0,
                                           in1=r3[:, t.slot], op0=ALU.mult, op1=ALU.mult).then_inc(shift3, 1)

        def low_xT(t):
            dve.wait_ge(xT_hi, t.n + 1)
            nc.vector.tensor_tensor(xnT[:, 1, :, tokens_of(t.n)],
                                    banks[:, 4 + t.slot, 0:DIM].rearrange("p (b n) -> p b n", b=DIM_BLOCKS),
                                    xnT[:, 0, :, tokens_of(t.n)], ALU.subtract).then_inc(xT_ready, 1)

        pipeline(dve, TILES, [(2, embed), (0, stats_of_pixels), (2, scale2), (1, low_zT(0)), (0, scale1),
                              (1, low_zT(1)), (2, tokens), (0, v_weights), (3, low_xT), (2, scale3)])

        def odd_keys(blocks):
            def stage(c):
                for b in blocks:
                    dve.wait_ge(proj_made, 8 * c.n + b + 1)
                    nc.vector.tensor_scalar(row64(c, b, 1), banks[KEY:P, b % 2, 0:CHUNK], 1 / W_SCALE, None,
                                            ALU.mult).then_inc(proj_odd, 1)
            return stage

        def centre(g):
            def stage(c):
                dve.wait_ge(score_made, 2 * c.n + g + 1)
                nc.vector.reduce_max(most[:, g], by_bank_head(scores_of(g)), axis=X).then_inc(most_ready, 1)
                dve.wait_ge(most_ready, 2 * c.n + g + 1)
                nc.vector.tensor_tensor(by_bank_head(prob[:, g]), by_bank_head(scores_of(g)),
                                        most[:, g].rearrange("p (b h) -> p b h", b=2).unsqueeze(3)
                                        .to_broadcast([P, 2, HEADS, TOKENS]), ALU.subtract).then_inc(centred, 1)
            return stage

        def totals(g):
            def stage(c):
                dve.wait_ge(exp_ready, 2 * c.n + g + 1)
                nc.vector.reduce_sum(total[:, g], by_head(prob[:, g]), axis=X).then_inc(total_ready, 1)
                dve.wait_ge(total_ready, 2 * c.n + g + 1)
                nc.vector.reciprocal(share[:, g], total[:, g]).then_inc(share_ready, 1)
            return stage

        def low_pieces(c):
            for s in range(2):
                dve.wait_ge(piece_hi, 2 * c.n + s + 1)
                at = w[:, bass.ds(2 * c.n + s, 1)].rearrange("p o l x -> p (o l) x")
                nc.vector.scalar_tensor_tensor(out=at[:, 1], in0=w_stage[:, s], scalar=W_SCALE, in1=at[:, 0],
                                               op0=ALU.mult, op1=ALU.subtract).then_inc(piece_ready, 1)

        pipeline(dve, CHUNKS, [(1, centre(0)), (0, odd_keys((0, 1))), (1, centre(1)), (0, odd_keys((2, 3))),
                               (1, totals(0)), (0, odd_keys((4, 5))), (1, totals(1)), (0, odd_keys((6, 7))),
                               (0, low_pieces)])

        def add_attention(t):
            dve.wait_ge(h0t_loaded[t.slot], 32 * (t.turn + 1))
            if t.reuses:
                dve.wait_ge(h1_stored[t.slot], 16 * t.turn)
                dve.wait_ge(xn_ready, t.n - 1)
            nc.vector.tensor_tensor(h1t[:, t.slot], h0t[:, t.slot], attn_t[:, t.slot], ALU.add).then_inc(h1_ready, 1)
            dve.wait_ge(h1_ready, t.n + 1)
            nc.vector.bn_stats(st4[:, t.slot], h1t[:, t.slot])
            dve.drain()
            nc.vector.bn_aggr(mv4[:, t.slot], st4[:, t.slot]).then_inc(aggr4, 1)

        def scale4(t):
            dve.wait_ge(std4, t.n + 1)
            nc.vector.reciprocal(r4[:, t.slot], sd4[:, t.slot]).then_inc(rcp4, 1)
            dve.wait_ge(rcp4, t.n + 1)
            nc.vector.scalar_tensor_tensor(out=nb4[:, t.slot], in0=mv4[:, t.slot, 0:1], scalar=-1.0,
                                           in1=r4[:, t.slot], op0=ALU.mult, op1=ALU.mult).then_inc(shift4, 1)

        def low_x4(t):
            dve.wait_ge(x4_hi, t.n + 1)
            nc.vector.tensor_tensor(xTs[:, 1, :, tokens_of(t.n)],
                                    banks[:, t.slot, 0:DIM].rearrange("p (b n) -> p b n", b=DIM_BLOCKS),
                                    xTs[:, 0, :, tokens_of(t.n)], ALU.subtract).then_inc(x4_ready, 1)

        def logits(t):
            dve.wait_ge(logit_made, t.n + 1)
            nc.vector.scalar_tensor_tensor(out=logit[:, bass.ds(t.n, 1)].rearrange("p o e -> p (o e)"),
                                           in0=banks[:, 2 + t.slot, 0:EXPERTS], scalar=1 / W_SCALE, in1=rb_row[:],
                                           op0=ALU.mult, op1=ALU.add).then_inc(logit_ready, 1)

        steps = [0]

        def next_step(instruction):
            instruction.then_inc(routed_step, 1)
            steps[0] += 1
            dve.wait_ge(routed_step, steps[0])

        def per_token(x):
            return x[:].unsqueeze(2).to_broadcast([P, TILES, EXPERTS])

        def per_expert(x):
            return x[:].unsqueeze(1).to_broadcast([P, TILES, EXPERTS])

        def one_hot(scores, maximum, most_code, hot):
            next_step(nc.vector.reduce_max(maximum[:], scores[:], axis=X))
            next_step(nc.vector.tensor_tensor(hit[:], scores[:], per_token(maximum), ALU.is_equal))
            next_step(nc.vector.tensor_tensor(code[:], hit[:], per_expert(rev), ALU.mult))
            next_step(nc.vector.reduce_max(most_code[:], code[:], axis=X))
            next_step(nc.vector.tensor_tensor(hot[:], per_expert(rev), per_token(most_code), ALU.is_equal))

        dve.wait_ge(router_hi, 1)
        nc.vector.scalar_tensor_tensor(out=wr_hl[:, 1], in0=wr32[:], scalar=W_SCALE, in1=wr_hl[:, 0],
                                       op0=ALU.mult, op1=ALU.subtract).then_inc(router_ready, 1)
        pipeline(dve, TILES, [(0, add_attention), (0, scale4), (2, low_x4), (3, logits)])
        dve.wait_ge(logit_ready, TILES)
        one_hot(logit, best, best_code, first_hot)
        next_step(nc.vector.scalar_tensor_tensor(out=logit2[:], in0=first_hot[:], scalar=TAKEN, in1=logit[:],
                                                 op0=ALU.mult, op1=ALU.add))
        one_hot(logit2, second, second_code, second_hot)
        nc.vector.tensor_tensor(gap[:], second[:], best[:], ALU.subtract).then_inc(gap_ready, 1)
        nc.vector.tensor_tensor(both_hot[:], first_hot[:], second_hot[:], ALU.add).then_inc(hot_ready, 1)

        def finish_routing(t):
            if t.step != 0:
                return
            dve.wait_ge(growth_ready, 1)
            next_step(nc.vector.tensor_scalar(gap[:], growth[:], 1.0, None, ALU.add))
            next_step(nc.vector.reciprocal(weight[:, 0], gap[:]))
            nc.vector.tensor_tensor(weight[:, 1], weight[:, 0], growth[:], ALU.mult).then_inc(weight_ready, 1)
            dve.wait_ge(rank_made, 1)
            next_step(nc.vector.tensor_scalar(cnt_i[:, 0], banks[:, 7, TILES * EXPERTS:(TILES + 1) * EXPERTS],
                                              FFN_TILE - 1.0, None, ALU.add))
            next_step(nc.vector.tensor_scalar(cnt_i[:, 1], cnt_i[:, 0], FFN_TILE.bit_length() - 1, None,
                                              ALU.logical_shift_right))
            next_step(nc.vector.tensor_copy(tiles_f[:], cnt_i[:, 1]))
            x, y = tiles_f, cum_a
            for reach in (1, 2, 4):
                nc.vector.tensor_copy(y[:, 0:reach], x[:, 0:reach])
                next_step(nc.vector.tensor_tensor(y[:, reach:], x[:, reach:], x[:, 0:EXPERTS - reach], ALU.add))
                x, y = y, cum_b if y is cum_a else cum_a
            next_step(nc.vector.tensor_copy(bounds[:], x[:]))
            next_step(nc.vector.tensor_tensor(start_row[:], x[:], tiles_f[:], ALU.subtract))
            next_step(nc.vector.scalar_tensor_tensor(
                out=where[:], in0=per_expert(start_row), scalar=float(FFN_TILE),
                in1=banks[:, 7, 0:TILES * EXPERTS].rearrange("p (t e) -> p t e", e=EXPERTS), op0=ALU.mult, op1=ALU.add))
            for choice, hot in enumerate((first_hot, second_hot)):
                next_step(nc.vector.tensor_tensor(code[:], hot[:], where[:], ALU.mult))
                next_step(nc.vector.reduce_sum(chosen[:, choice], code[:], axis=X))
            nc.vector.tensor_copy(pos[:], chosen[:]).then_inc(pos_ready, 1)

        def low_xh(t):
            dve.wait_ge(xh_hi, t.k + 1)
            nc.vector.tensor_tensor(xh[:, t.slot, 1].rearrange("p b n -> p (b n)"), banks[:, 0],
                                    xh[:, t.slot, 0].rearrange("p b n -> p (b n)"), ALU.subtract).then_inc(xh_ready, 1)

        def products(q, width):
            def stage(t):
                step, s = 3 * t.n + q, (t.slot + q) % 2
                dve.wait_ge(silu_ready, step + 1)
                if t.step is None or t.n > 0 or q == 2:
                    dve.wait_ge(hT_ready, step - 1)
                ups = banks[:, 3 + s].rearrange("p (b n) -> p b n", b=2)[:, :, 0:width]
                into = prod[:, s].rearrange("p (b n) -> p b n", b=2)[:, :, 0:width]
                gate = silu[:, s].rearrange("p (b n) -> p b n", b=2)[:, :, 0:width]
                if q < 2:
                    last = nc.vector.scalar_tensor_tensor(out=into, in0=ups, scalar=H_SCALE / W_SCALE, in1=gate,
                                                          op0=ALU.mult, op1=ALU.mult)
                else:
                    nc.vector.scalar_tensor_tensor(out=into[:, 0], in0=ups[:, 0], scalar=H_SCALE / W_SCALE,
                                                   in1=gate[:, 0], op0=ALU.mult, op1=ALU.mult)
                    last = nc.vector.scalar_tensor_tensor(
                        out=into[0:P // 2, 1], in0=banks[P // 2:P, 1 + s, FFN_TILE:FFN_TILE + width],
                        scalar=H_SCALE / W_SCALE, in1=gate[0:P // 2, 1], op0=ALU.mult, op1=ALU.mult)
                last.then_inc(prod_ready, 1)
            return stage

        def low_hT(q, width):
            def stage(t):
                step, s = 3 * t.n + q, (t.slot + q) % 2
                dve.wait_ge(hT_hi, step + 1)
                nc.vector.tensor_tensor(hT[:, t.slot, 1, 2 * q:2 * q + 2, 0:width],
                                        prod[:, s].rearrange("p (b n) -> p b n", b=2)[:, :, 0:width],
                                        hT[:, t.slot, 0, 2 * q:2 * q + 2, 0:width], ALU.subtract).then_inc(hT_ready, 1)
            return stage

        def shared_results(phase):
            halves = PHASES[phase][2] // P

            def stage(t):
                dve.wait_ge(down_made, t.n + 1)
                dve.wait_ge(xg_loaded[phase][t.slot], 16 * (t.k_turn + 1))
                if t.step is None or t.n >= 2:
                    dve.wait_ge(y_stored[t.slot], 16 * t.turn)
                nc.vector.scalar_tensor_tensor(out=yo[:, t.slot, 0:halves], in0=banks[:, 5:5 + halves, 0:DIM],
                                               scalar=1 / (W_SCALE * H_SCALE), in1=xg[:, t.slot, 0:halves],
                                               op0=ALU.mult, op1=ALU.add).then_inc(y_out, 1)
            return stage

        def low_late_pieces(t):
            for n in LATE_AT.get(t.step, ()):
                late = n - LATE_FIRST
                dve.wait_ge(late_hi, late + 1)
                nc.vector.scalar_tensor_tensor(out=w[:, n, 1], in0=w_stage[:, late % 2], scalar=W_SCALE, in1=w[:, n, 0],
                                               op0=ALU.mult, op1=ALU.subtract).then_inc(late_ready, 1)

        def combine(t):
            dve.wait_ge(gathered[t % 2], 32 * (t // 2 + 1))
            dve.wait_ge(base_loaded[t % 2], 16 * (t // 2 + 1))
            if t >= 2:
                dve.wait_ge(out_stored[t % 2], 16 * (t // 2))
            nc.vector.scalar_tensor_tensor(out=mixed[:, t % 2], in0=picked[:, t % 2, 0], scalar=weight[:, 0, t:t + 1],
                                           in1=base_t[:, t % 2], op0=ALU.mult, op1=ALU.add).then_inc(half_mixed, 1)
            dve.wait_ge(half_mixed, t + 1)
            nc.vector.scalar_tensor_tensor(out=mixed[:, t % 2], in0=picked[:, t % 2, 1], scalar=weight[:, 1, t:t + 1],
                                           in1=mixed[:, t % 2], op0=ALU.mult, op1=ALU.add).then_inc(mixed_ready, 1)

        for phase, (kind, count, width) in enumerate(PHASES):
            routed = kind == "routed"
            before = [(0, low_xh)] if routed else []
            late = [(0, low_late_pieces)] if phase == 0 else []
            routing = [(1, finish_routing)] if phase == 0 else []
            after = [] if routed else [(2, shared_results(phase))]
            pipeline(dve, count, [(1, products(0, width)), (1, low_hT(0, width))] + after + [
                (1, products(1, width)), (1, low_hT(1, width))] + before + late + [
                (1, products(2, width)), (1, low_hT(2, width))] + routing, STARTS[phase], phase == 0)
        dve.wait_ge(weight_ready, 1)
        for t in range(TILES):
            combine(t)

    PRODUCTS = ((0, 0), (0, 1), (1, 0))

    @block.tensor
    def _(pe):
        def bias_product(t):
            if t.first:
                pe.wait_ge(b1_wide, 1)
                pe.wait_ge(wtok_loaded, 32)
                for b in range(PIX_BLOCKS):
                    last = nc.tensor.matmul(banks[:, 7, 0:DIM], b1wide[:, b], wtok32[:, b], start=b == 0,
                                            stop=b == PIX_BLOCKS - 1)
                last.then_inc(bias_made, 1)

        pe.wait_ge(ident_ready, 2)

        def transpose_z(t):
            pe.wait_ge(z_ready, t.n + 1)
            for half in range(2):
                if not t.first:
                    pe.wait_ge(zT_ready, 2 * t.n + half - 1)
                for b in range(THIRD):
                    last = nc.tensor.transpose(banks[:, half, P * b:P * b + P],
                                               z[:, t.slot, P * (THIRD * half + b):P * (THIRD * half + b) + P], ident[:])
                last.then_inc(zT_made, 1)

        def embed(t):
            pe.wait_ge(zT_ready, 2 * t.n + 2)
            if t.first:
                pe.wait_ge(wtok_ready, 1)
                pe.wait_ge(rows_ready, 1)
            if t.reuses:
                pe.wait_ge(h0_ready, t.n - 1)
            bank = 2 + t.slot
            for b in range(PIX_BLOCKS):
                for zp, wp in PRODUCTS:
                    nc.tensor.matmul(banks[:, bank, 0:DIM], zT[:, t.slot, zp, P * b:P * b + P], wtok[:, wp, b],
                                     start=b == 0 and (zp, wp) == (0, 0), stop=b == PIX_BLOCKS - 1 and zp == 1)
            for part in range(2):
                last = nc.tensor.matmul(banks[:, bank, DIM:2 * DIM], pick40[:, tokens_of(t.n)], rows_hl[:, part],
                                        start=part == 0, stop=part == 1)
            last.then_inc(y_made, 1)

        def transpose_x(t):
            pe.wait_ge(xn0_ready, t.n + 1)
            if t.reuses:
                pe.wait_ge(xT_ready, t.n - 1)
            for b in range(DIM_BLOCKS):
                last = nc.tensor.transpose(banks[:, 4 + t.slot, P * b:P * b + P], xn0[:, t.slot, P * b:P * b + P], ident[:])
            last.then_inc(xT_made, 1)

        def values(t):
            pe.wait_ge(xT_ready, t.n + 1)
            if t.first:
                pe.wait_ge(m_ready, 1)
                pe.wait_ge(bias_ready, 1)
            if t.reuses:
                pe.wait_ge(v_ready, t.n - 1)
            for b in range(DIM_BLOCKS):
                for xp, mp in PRODUCTS:
                    last = nc.tensor.matmul(banks[:, 6 + t.slot, 0:DIM], xnT[:, xp, b, tokens_of(t.n)], mv[:, mp, b],
                                            start=b == 0 and (xp, mp) == (0, 0), stop=b == DIM_BLOCKS - 1 and xp == 1)
            last.then_inc(v_made, 1)

        pipeline(pe, TILES, [(0, bias_product), (1, transpose_z), (3, transpose_x), (1, embed), (3, values)])

        def project(c):
            for b in range(8):
                if b >= 2 or not c.first:
                    pe.wait_ge(proj_even, 8 * c.n + b - 1)
                    pe.wait_ge(proj_odd, 8 * c.n + b - 1)
                for d in range(DIM_BLOCKS):
                    for mp, xp in PRODUCTS:
                        last = nc.tensor.matmul(banks[:, b % 2, 0:CHUNK], mqk[:, mp, d, P * b:P * b + P],
                                                xnT[:, xp, d, bass.ds(c.n * CHUNK, CHUNK)],
                                                start=d == 0 and (mp, xp) == (0, 0), stop=d == 1 and mp == 1)
                last.then_inc(proj_made, 1)

        def score(c):
            pe.wait_ge(proj_even, 8 * c.n + 8)
            pe.wait_ge(proj_odd, 8 * c.n + 8)
            for g in range(2):
                if not c.first:
                    pe.wait_ge(centred, 2 * c.n + g - 1)
                pe.sem_inc(score_begun, 1)
                for pair in range(2):
                    for b in range(2):
                        for h in range(HEADS):
                            at = (4 * g + 2 * pair + b) * IMAGE64 + TOKENS * h
                            last = nc.tensor.matmul(
                                banks[KEY * b:KEY * b + KEY, 2 + 2 * g + pair, TOKENS * h:TOKENS * h + TOKENS],
                                k64[:, c.slot, at:at + KEY], q64[:, c.slot, at:at + TOKENS], start=True, stop=True)
                last.then_inc(score_made, 1)

        def mix(c):
            pe.wait_ge(vbd_loaded[c.slot], 16 * 8 * (c.turn + 1))
            for g in range(2):
                pe.wait_ge(prob_ready, 2 * c.n + g + 1)
                for pair in range(2):
                    if g or not c.first:
                        pe.wait_ge(o_ready, 4 * c.n + 2 * g + pair - 1)
                    for h in range(HEADS):
                        last = nc.tensor.matmul(
                            banks[0:TOKENS, 6 + pair, 2 * VAL * h:2 * VAL * h + 2 * VAL],
                            prob[:, g, pair, h:IMAGE64:HEADS],
                            vbd[:, c.slot, 2 * g + pair, h].rearrange("p b d -> p (b d)"), start=True, stop=True)
                    last.then_inc(o_made, 1)

        pe.wait_ge(m_qk_ready, 1)
        pe.wait_ge(pad_zero, 1)
        pe.wait_ge(h0_ready, TILES)
        pe.wait_ge(v_ready, TILES)
        pipeline(pe, CHUNKS, [(0, project), (1, mix), (0, score)])

        def transpose_x4(t):
            pe.wait_ge(xn_ready, t.n + 1)
            if t.reuses:
                pe.wait_ge(x4_ready, t.n - 1)
            for b in range(DIM_BLOCKS):
                last = nc.tensor.transpose(banks[:, t.slot, P * b:P * b + P],
                                           xn4[:, t.slot, P * b:P * b + P], ident[:])
            last.then_inc(x4_made, 1)

        def router(t):
            pe.wait_ge(x4_ready, t.n + 1)
            if t.first:
                pe.wait_ge(router_ready, 1)
            if t.reuses:
                pe.wait_ge(logit_ready, t.n - 1)
            for b in range(DIM_BLOCKS):
                for xp, rp in PRODUCTS:
                    last = nc.tensor.matmul(banks[:, 2 + t.slot, 0:EXPERTS], xTs[:, xp, b, tokens_of(t.n)],
                                            wr_hl[:, rp, b], start=b == 0 and (xp, rp) == (0, 0),
                                            stop=b == DIM_BLOCKS - 1 and xp == 1)
            last.then_inc(logit_made, 1)

        pe.wait_ge(proj_even, 8 * CHUNKS)
        pe.wait_ge(proj_odd, 8 * CHUNKS)
        pe.wait_ge(centred, 2 * CHUNKS)
        pe.wait_ge(o_ready, 4 * CHUNKS)
        pipeline(pe, TILES, [(1, transpose_x4), (2, router)])

        def rank(t):
            if t.step != 0:
                return
            pe.wait_ge(hot_ready, 1)
            for back in range(TILES):
                nc.tensor.matmul(banks[:, 7, EXPERTS * back:EXPERTS * TILES], ones[:] if back else slt[:],
                                 both_hot[:, 0:TILES - back].rearrange("p t e -> p (t e)"),
                                 start=back == 0, stop=back == TILES - 1, skip_group_check=True)
            for t in range(TILES):
                last = nc.tensor.matmul(banks[:, 7, EXPERTS * TILES:EXPERTS * (TILES + 1)], ones[:], both_hot[:, t],
                                        start=t == 0, stop=t == TILES - 1)
            last.then_inc(rank_made, 1)

        def transpose_routed(t):
            pe.wait_ge(xg_loaded[1][t.slot], 16 * (t.k_turn + 1))
            if t.step is None or t.step >= 1:
                pe.wait_ge(xh_ready, t.k)
            for b in range(DIM_BLOCKS):
                for half in range(2):
                    last = nc.tensor.transpose(banks[:, 0, FFN_TILE * b + P * half:FFN_TILE * b + P * half + P],
                                               xg[:, t.slot, half, P * b:P * b + P], ident[:])
            last.then_inc(xT4_made, 1)

        def expert_pieces(phase, t):
            if PHASES[phase][0] == "shared":
                return lambda piece, part, cols, rows=P: w[0:rows, piece, part, cols]
            e = (ends[0] <= t.k)
            for end in ends[1:]:
                e = e + (end <= t.k)
            first = nc.snap(3 * e + 3)
            return lambda piece, part, cols, rows=P: w[0:rows, bass.ds(first + piece, 1), part, cols].rearrange("p o x -> p (o x)")

        current = {}

        def gate_up(phase, q):
            kind, _, width = PHASES[phase]

            def stage(t):
                step, s = 3 * t.n + q, (t.slot + q) % 2
                if q == 0:
                    current["pieces"] = expert_pieces(phase, t)
                    if kind == "routed":
                        pe.wait_ge(xh_ready, t.k + 1)
                pieces = current["pieces"]
                if t.step is None or t.n > 0 or q == 2:
                    pe.wait_ge(prod_ready, step - 1)
                for bank, cols, blocks in ((1 + s, GATES[q], 2), (3 + s, UPS[q], 2 if q < 2 else 1)):
                    for block in range(blocks):
                        for d in range(DIM_BLOCKS):
                            for wp, xp in PRODUCTS:
                                x = (xh[:, t.slot, xp, d] if kind == "routed" else
                                     xTs[:, xp, d, bass.ds(t.k * width + FIRST_TOKEN[phase], width)])
                                last = nc.tensor.matmul(
                                    banks[:, bank, FFN_TILE * block:FFN_TILE * block + width],
                                    pieces(d, wp, slice(cols + P * block, cols + P * block + P)), x,
                                    start=d == 0 and (wp, xp) == (0, 0), stop=d == 1 and wp == 1)
                last.then_inc(gu_made, 1)
            return stage

        def down(phase, q):
            kind, _, width = PHASES[phase]

            def stage(t):
                pieces = expert_pieces(phase, t) if q == 2 else current["pieces"]
                pe.wait_ge(hT_ready, 3 * t.n + q + 1)
                if q == 0 and (t.step is None or t.n > 0):
                    pe.wait_ge(y_out, t.n)
                for block in (2 * q, 2 * q + 1):
                    rows = P if block < 5 else P // 2
                    for half in range(width // P):
                        for hp, wp in PRODUCTS:
                            last = nc.tensor.matmul(banks[:, 5 + half, 0:DIM],
                                                    hT[0:rows, t.slot, hp, block, P * half:P * half + P],
                                                    pieces(2, wp, slice(DIM * block, DIM * block + DIM), rows),
                                                    start=block == 0 and (hp, wp) == (0, 0), stop=block == 5 and hp == 1,
                                                    skip_group_check=True)
                if q == 2:
                    last.then_inc(down_made, 1)
            return stage

        pe.wait_ge(logit_ready, TILES)
        ends = []
        for phase, (kind, count, _) in enumerate(PHASES):
            if kind == "routed":
                pe.wait_ge(late_ready, PIECES - LATE_FIRST)
                pe.wait_ge(pos_ready, 1)
                ends = [nc.values_load(bounds[0:1, e:e + 1], engines=[pe.engine], min_val=0, max_val=SLOT_TILES,
                                       skip_runtime_bounds_check_because="they are sums of tile counts")
                        for e in range(ROUTED - 1)]
            before = [(0, transpose_routed)] if kind == "routed" else []
            ranks = [(1, rank)] if phase == 0 else []
            pipeline(pe, count, [(1, gate_up(phase, 0)), (2, down(phase, 2)), (1, gate_up(phase, 1)),
                                 (1, down(phase, 0))] + before + [(1, gate_up(phase, 2)), (1, down(phase, 1))]
                     + ranks, STARTS[phase], phase == 0)

    ctx.close()


def laid_out(i):
    f = lambda name: np.asarray(i[name])
    zeros = lambda *shape: np.zeros(shape, np.float32)
    by_block = lambda m: np.ascontiguousarray(m.reshape(-1, P, m.shape[-1]).transpose(1, 0, 2))
    x = f("x").reshape(IMAGES, CHANNELS, GRID, PATCH, GRID, PATCH).transpose(0, 2, 4, 3, 5, 1)
    patches = zeros(IMAGES, TOKENS, PIXELS)
    patches[:, 2:] = x.reshape(IMAGES, GRID * GRID, PIXELS)
    yy, xx = np.meshgrid(np.arange(GRID), np.arange(GRID), indexing="ij")
    omega = np.arange(DIM // 4, dtype=np.float32) / np.float32(DIM // 4 - 1)
    omega = (np.float32(1.0) / np.float32(10000.0) ** omega).astype(np.float32)
    yo = yy.reshape(-1)[:, None].astype(np.float32) * omega
    xo = xx.reshape(-1)[:, None].astype(np.float32) * omega
    pe = np.concatenate([np.sin(xo), np.cos(xo), np.sin(yo), np.cos(yo)], axis=1).astype(np.float32)
    rows = np.concatenate([pe, f("L0_tok_ln2_b")[None], f("cls_tok")[0], f("L0_tok_cls_token")[0],
                           f("L0_tok_cls_pos_embedding")[0]], axis=0)
    pick = np.zeros((PICKED, IMAGES, TOKENS), np.float16)
    for r in range(GRID * GRID):
        pick[r, :, 2 + r] = 1
    pick[36, :, 2:] = 1
    pick[37, :, 0] = 1
    pick[38:40, :, 1] = 1
    gate = np.concatenate([f("L0_ffn_sg")[None], f("L0_ffn_rg")]).transpose(0, 2, 1)
    up = np.concatenate([f("L0_ffn_su")[None], f("L0_ffn_ru")]).transpose(0, 2, 1)
    down = np.concatenate([f("L0_ffn_sd")[None], f("L0_ffn_rd")]).transpose(0, 2, 1)
    pieces = zeros(EXPERTS, 3, P, PIECE)
    order = [gate[..., 0:256], up[..., 0:256], gate[..., 256:512], up[..., 256:512], gate[..., 512:704],
             up[..., 640:704], up[..., 512:640]]
    gate_up = np.concatenate(order, axis=2)
    pieces[:, 0, :, :2 * INNER] = gate_up[:, :P]
    pieces[:, 1, :, :2 * INNER] = gate_up[:, P:]
    padded = zeros(EXPERTS, 6 * P, DIM)
    padded[:, :INNER] = down
    pieces[:, 2] = padded.reshape(EXPERTS, 6, P, DIM).transpose(0, 2, 1, 3).reshape(EXPERTS, P, 6 * DIM)
    pieces = pieces.reshape(PIECES, P, PIECE)
    router = zeros(P, DIM_BLOCKS, EXPERTS)
    router[..., :ROUTED] = f("L0_ffn_wr").T.reshape(DIM_BLOCKS, P, ROUTED).transpose(1, 0, 2)
    router_bias = np.full(EXPERTS, NEVER, np.float32)
    router_bias[:ROUTED] = f("L0_ffn_rb")
    is_patch = np.ones((IMAGES, TOKENS), np.float32)
    is_patch[:, :2] = 0
    return {
        "patches": patches.reshape(TILES, P, PIXELS),
        "w_tok": by_block(f("L0_tok_W")),
        "ln1_g": np.ascontiguousarray(f("L0_tok_ln1_g").reshape(PIX_BLOCKS, P).T),
        "ln1_b": np.ascontiguousarray(f("L0_tok_ln1_b").reshape(PIX_BLOCKS, P).T),
        "tok_bias": f("L0_tok_bias"), "ln2_g": f("L0_tok_ln2_g"),
        "rows40": rows, "pick40": pick.reshape(PICKED, ROWS),
        "is_patch": np.ascontiguousarray(is_patch.reshape(TILES, P).T),
        "Mv": by_block(f("L0_attn_Mv")),
        "Mqk": by_block(np.concatenate([f("L0_attn_Mq"), f("L0_attn_Mk")], axis=1)),
        "pieces": pieces,
        "router": router, "router_bias": router_bias,
        "rev": np.arange(EXPERTS, 0, -1, dtype=np.float32),
        "slt": np.triu(np.ones((P, P), np.float16), 1), "ones": np.ones((P, P), np.float16),
    }


def kernel(**inputs):
    from concourse import bacc
    from concourse.bass_utils import run_bass_kernel_spmd

    arrays = {f"in_{name}": np.ascontiguousarray(v) for name, v in laid_out(inputs).items()}
    nc = bacc.Bacc("TRN2", target_bir_lowering=False, num_devices=1)
    a = {name[3:]: nc.dram_tensor(name, v.shape, mybir.dt.from_np(v.dtype), kind="ExternalInput").ap()
         for name, v in arrays.items()}
    out = nc.dram_tensor("out", (IMAGES, TOKENS, DIM), F32, kind="ExternalOutput").ap()
    program(nc, a, out.rearrange("i t d -> (i t) d"))
    return run_bass_kernel_spmd(nc, [arrays], core_ids=[0]).results[0]["out"]
```
